# Optimizing a Trainium2 kernel written in Bass

```python
import numpy as np
import jax
import jax.numpy as jnp

def _softmax(x, axis=-1):
    return jax.nn.softmax(x, axis=axis)

def _gelu(x):
    return jax.nn.gelu(x, approximate=True)

def _silu(x):
    return jax.nn.silu(x)

def _sigmoid(x):
    return jax.nn.sigmoid(x)

def _layernorm(x, axis=-1, eps=1e-05):
    m = jnp.mean(x, axis=axis, keepdims=True)
    v = jnp.var(x, axis=axis, keepdims=True)
    return (x - m) / jnp.sqrt(v + eps)

def _scatter_add(tgt, idx, src, axis=0):
    return tgt.at[idx].add(src)

def _segment_sum(src, seg, n):
    return jax.ops.segment_sum(src, seg, n)
kernel_name = 'mk_seq_postln_d1_jaxref_r8_7b682f'

def setup_inputs(seed: int=0):
    np.random.seed(seed)
    _w = jnp.asarray

    def _L0_attn_setup():
        import jax, jax.numpy as jnp
        import numpy as np
        D_MODEL = 128
        NUM_HEADS = 16
        D_K = D_MODEL // NUM_HEADS
        ROPE_THETA = 10000.0

        def _apply_rope(t):
            S, dk = (t.shape[-2], t.shape[-1])
            inv_freq = 1.0 / ROPE_THETA ** (jnp.arange(0, dk, 2) / dk)
            angles = jnp.outer(jnp.arange(S), inv_freq)
            cos = jnp.repeat(jnp.cos(angles), 2, axis=-1).astype(t.dtype)
            sin = jnp.repeat(jnp.sin(angles), 2, axis=-1).astype(t.dtype)
            t_even = t[..., 0::2]
            t_odd = t[..., 1::2]
            t_rot = jnp.stack([-t_odd, t_even], axis=-1).reshape(t.shape)
            return t * cos + t_rot * sin
        key = jax.random.key(seed)
        kx, kq, kk, kv, ko = jax.random.split(key, 5)
        B, S = (4, 256)
        std = (2.0 / (D_MODEL + D_MODEL)) ** 0.5

        def w(k):
            return jax.random.truncated_normal(k, -3.0, 3.0, (D_MODEL, D_MODEL), jnp.float32) * std
        return {'x': jax.random.normal(kx, (B, S, D_MODEL), jnp.float32), 'Wq': w(kq), 'Wk': w(kk), 'Wv': w(kv), 'Wo': w(ko)}
    _L0_attn_in = _L0_attn_setup()

    def _L0_ffn_setup():
        import jax, jax.numpy as jnp
        import numpy as np
        D, H, E, K, S = (128, 256, 8, 2, 1)
        B, L = (4, 256)
        key = jax.random.key(seed)
        ks = jax.random.split(key, 9)
        std = 0.02
        return {'x': jax.random.normal(ks[0], (B, L, D), dtype=jnp.float32), 'router_w': jax.random.normal(ks[1], (E, D), dtype=jnp.float32) * std, 'experts_bias': jnp.zeros((E,), dtype=jnp.float32), 'w1': jax.random.normal(ks[2], (E, D, H), dtype=jnp.float32) * std, 'w3': jax.random.normal(ks[3], (E, D, H), dtype=jnp.float32) * std, 'w2': jax.random.normal(ks[4], (E, H, D), dtype=jnp.float32) * std, 'sw1': jax.random.normal(ks[5], (S, D, H), dtype=jnp.float32) * std, 'sw3': jax.random.normal(ks[6], (S, D, H), dtype=jnp.float32) * std, 'sw2': jax.random.normal(ks[7], (S, H, D), dtype=jnp.float32) * std}
    _L0_ffn_in = _L0_ffn_setup()
    _d = {'L0_attn_x': _L0_attn_in['x'], 'L0_attn_Wq': _L0_attn_in['Wq'], 'L0_attn_Wk': _L0_attn_in['Wk'], 'L0_attn_Wv': _L0_attn_in['Wv'], 'L0_attn_Wo': _L0_attn_in['Wo'], 'L0_ffn_router_w': _L0_ffn_in['router_w'], 'L0_ffn_experts_bias': _L0_ffn_in['experts_bias'], 'L0_ffn_w1': _L0_ffn_in['w1'], 'L0_ffn_w3': _L0_ffn_in['w3'], 'L0_ffn_w2': _L0_ffn_in['w2'], 'L0_ffn_sw1': _L0_ffn_in['sw1'], 'L0_ffn_sw3': _L0_ffn_in['sw3'], 'L0_ffn_sw2': _L0_ffn_in['sw2']}
    _x0 = _d['L0_attn_x']
    _d['L0_attn_x'] = jax.random.normal(jax.random.fold_in(jax.random.key(seed), 1), (8, 512, 128), dtype=_x0.dtype)
    del _x0
    return _d

def reference(L0_attn_x, L0_attn_Wq, L0_attn_Wk, L0_attn_Wv, L0_attn_Wo, L0_ffn_router_w, L0_ffn_experts_bias, L0_ffn_w1, L0_ffn_w3, L0_ffn_w2, L0_ffn_sw1, L0_ffn_sw3, L0_ffn_sw2):

    def _L0_attn_ref(x, Wq, Wk, Wv, Wo):
        import jax, jax.numpy as jnp
        import numpy as np
        D_MODEL = 128
        NUM_HEADS = 16
        D_K = D_MODEL // NUM_HEADS
        ROPE_THETA = 10000.0

        def _apply_rope(t):
            S, dk = (t.shape[-2], t.shape[-1])
            inv_freq = 1.0 / ROPE_THETA ** (jnp.arange(0, dk, 2) / dk)
            angles = jnp.outer(jnp.arange(S), inv_freq)
            cos = jnp.repeat(jnp.cos(angles), 2, axis=-1).astype(t.dtype)
            sin = jnp.repeat(jnp.sin(angles), 2, axis=-1).astype(t.dtype)
            t_even = t[..., 0::2]
            t_odd = t[..., 1::2]
            t_rot = jnp.stack([-t_odd, t_even], axis=-1).reshape(t.shape)
            return t * cos + t_rot * sin
        B, S, D = x.shape
        H, dk = (NUM_HEADS, D_K)
        q = jnp.einsum('bsi,io->bso', x, Wq).reshape(B, S, H, dk).swapaxes(1, 2)
        k = jnp.einsum('bsi,io->bso', x, Wk).reshape(B, S, H, dk).swapaxes(1, 2)
        v = jnp.einsum('bsi,io->bso', x, Wv).reshape(B, S, H, dk).swapaxes(1, 2)
        q = _apply_rope(q)
        k = _apply_rope(k)
        scores = jnp.einsum('bhqd,bhkd->bhqk', q, k) / dk ** 0.5
        causal = jnp.tril(jnp.ones((S, S), dtype=bool))
        scores = jnp.where(causal, scores, -jnp.inf)
        attn = jax.nn.softmax(scores, axis=-1)
        out = jnp.einsum('bhqk,bhkd->bhqd', attn, v)
        out = out.swapaxes(1, 2).reshape(B, S, D)
        return jnp.einsum('bsi,io->bso', out, Wo)

    def _L0_ffn_ref(x, router_w, experts_bias, w1, w3, w2, sw1, sw3, sw2):
        import jax, jax.numpy as jnp
        import numpy as np
        D, H, E, K, S = (128, 256, 8, 2, 1)
        B, L = (4, 256)
        b, l, d = x.shape
        xf = x.reshape(-1, d)
        sg = jnp.einsum('td,sdh->tsh', xf, sw1)
        su = jnp.einsum('td,sdh->tsh', xf, sw3)
        shared_out = jnp.einsum('tsh,shd->td', jax.nn.silu(sg) * su, sw2)
        logits = xf @ router_w.T + experts_bias
        rw, sel = jax.lax.top_k(logits, K)
        rw = jax.nn.softmax(rw.astype(jnp.float32), axis=-1).astype(x.dtype)
        cw = (jax.nn.one_hot(sel, E, dtype=x.dtype) * rw[..., None]).sum(axis=1)
        g = jnp.einsum('td,edh->teh', xf, w1)
        u = jnp.einsum('td,edh->teh', xf, w3)
        eo = jax.nn.silu(g) * u
        moe_out = jnp.einsum('te,teh,ehd->td', cw, eo, w2)
        return (moe_out + shared_out).reshape(b, l, d)
    x = L0_attn_x
    x = _layernorm(x + _L0_attn_ref(x, L0_attn_Wq, L0_attn_Wk, L0_attn_Wv, L0_attn_Wo), axis=-1)
    x = _layernorm(x + _L0_ffn_ref(x, L0_ffn_router_w, L0_ffn_experts_bias, L0_ffn_w1, L0_ffn_w3, L0_ffn_w2, L0_ffn_sw1, L0_ffn_sw3, L0_ffn_sw2), axis=-1)
    return x

_drawn_inputs = setup_inputs


def setup_inputs(seed=0):
    import zlib

    import numpy as np

    out = dict(_drawn_inputs(seed))
    spreads = {'L0_ffn_experts_bias': (0.0, 0.8)}
    factors = {'L0_ffn_router_w': 8.0,
     'L0_ffn_w1': 8.0,
     'L0_ffn_w3': 8.0,
     'L0_ffn_w2': 8.0,
     'L0_ffn_sw1': 6.965,
     'L0_ffn_sw3': 6.879,
     'L0_ffn_sw2': 6.885}
    for name, (base, spread) in spreads.items():
        noise = np.random.default_rng([zlib.crc32(name.encode()), seed]).standard_normal(out[name].shape)
        drawn = base * np.exp(spread * noise) if base else spread * noise
        out[name] = jnp.asarray(drawn.astype(out[name].dtype))
    for name, factor in factors.items():
        out[name] = (out[name] * factor).astype(out[name].dtype)
    return out
```

```python
from contextlib import ExitStack

import concourse.bass as bass
from concourse import mybir

ALU = mybir.AluOpType
ACT = mybir.ActivationFunctionType
F32 = mybir.dt.float32
BF16 = mybir.dt.bfloat16
U32 = mybir.dt.uint32
AX_X = mybir.AxisListType.X

P = 128
NEG = -3.0e38
EPS = 1e-5
SLOTS = [(0, 0), (0, 1), (1, 0), (1, 1), (0, 2), (2, 0)]


def build_block(nc, x, wq, wk, wv, wo, cos, sin, ident, mask, iota, router, bias,
                w1, w3, w2, sw1, sw3, sw2, out):
    B, S, D = x.shape
    E, _, HID = w1.shape
    H = 16
    DK = D // H
    T = S // P
    SCALE = float(DK) ** -0.5
    HALVES = HID // P
    NE = E + 1
    CH = NE * HALVES
    KS = DK * len(SLOTS)
    KZ = 96
    KM = KZ + 3
    PER_PV = 4

    RING = 4
    MAX_UNITS = []
    for i in range(T):
        stride = {0: 128, 1: 256, 2: 512, 3: 512}[i]
        n = S // stride
        MAX_UNITS += [(i, h, n, stride) for h in range(0, H, n)]
    NA = len(MAX_UNITS)
    PAIRS = H // 2
    PAIR_UNITS = [[(0, 1, 0), (0, 3, 3 * P)], [(0, 0, 0)], [(1, 1, 0), (1, 3, 3 * P)], [(1, 0, 0)],
                  [(0, 2, 0), (1, 2, 2 * P)]]
    NU = len(PAIR_UNITS)
    NB = NU * PAIRS
    GROUPS = H // PER_PV
    UPG = NB // GROUPS
    PRING = 2 * UPG
    assert NA % RING == 0 and NB % RING == 0

    def steps(attention, project_next, ffn):
        regions = []
        if attention:
            regions.append([("max", u) for u in range(NA)] + [("max_rows", 0)])
            if project_next:
                regions[0] += [("x_T", 0), ("project", 0), ("rope", 0), ("rest", 0)]
            line = []
            for g in range(GROUPS):
                line += [("scores", v) for v in range(UPG * g, UPG * (g + 1))]
                if g == 0 and project_next:
                    line[2:2] = [("low", 0)]
                if g >= 1:
                    line.insert(len(line) - UPG + 4, ("values", g - 1))
            regions.append(line)
            line = [("values", GROUPS - 1), ("heads_T", 0)]
            if project_next:
                line += [("v", 0)]
            regions.append(line + [("norm", 0), ("out_T", 0), ("out", 0), ("ln1_stats", 0), ("ln1", 0)])
        if not ffn:
            return [item for line in regions for item in line]
        events = [(1000 * r + k, item) for r, line in enumerate(regions) for k, item in enumerate(line)]
        add = lambda k, item: events.append((k, item))
        if attention:
            add(3.5, ("x1_T", 0)); add(5.5, ("router", 0))
            where, lag = [], []
            for r, (first, last, n, step) in enumerate(UPS):
                where += [1000 * r + first + (last - first) * k / max(n - 1, 1) for k in range(n)]
                lag += [step] * n
        else:
            add(-2, ("x1_T", 0)); add(-1, ("router", 0))
            where, lag = [3.0 * c for c in range(CH)], [1.0] * CH
        assert len(where) == CH
        for c, (k, step) in enumerate(zip(where, lag)):
            add(k + 0.01, ("up", c)); add(k + step + 0.02, ("tanh", c)); add(k + 2 * step + 0.03, ("glu", c))
            if c % HALVES == HALVES - 1:
                add(k + 3 * step + 0.04, ("down", c // HALVES)); add(k + 4 * step + 0.05, ("scale", c // HALVES))
        end = max(k for k, _ in events)
        add(end + 1, ("ln2_stats", 0)); add(end + 2, ("ln2", 0))
        return [item for _, item in sorted(events, key=lambda e: e[0])]

    UPS = [(8.5, 47.5, 5, 2.0), (2.5, 42.0, 10, 1.5), (0.5, 5.5, 3, 0.6)]

    with ExitStack() as ctx:
        def sb(name, shape, dt=F32):
            return ctx.enter_context(nc.sbuf_tensor(name, shape, dt))

        def sem(name):
            return ctx.enter_context(nc.semaphore(name))

        wq_sb = sb("wq_sb", [P, D]); wk_sb = sb("wk_sb", [P, D]); wv_sb = sb("wv_sb", [P, D])
        wo_sb = sb("wo_sb", [P, D])
        wqr_sb = sb("wqr_sb", [P, D]); wkr_sb = sb("wkr_sb", [P, D])
        cos_sb = sb("cos_sb", [P, S]); sin_sb = sb("sin_sb", [P, S])
        ident_sb = sb("ident_sb", [P, P]); mask_f = sb("mask_f", [P, P])
        ident_bf = sb("ident_bf", [P, P], BF16); mask_bf = sb("mask_bf", [P, P], BF16)
        iota_sb = sb("iota_sb", [P, E]); bias_sb = sb("bias_sb", [P, E]); router_sb = sb("router_sb", [P, E])
        w1_sb = sb("w1_sb", [P, NE, HID]); w3_sb = sb("w3_sb", [P, NE, HID])
        w2_sb = sb("w2_sb", [P, NE, HALVES, D])
        minus_half = sb("minus_half", [P, T])
        x_t = sb("x_t", [P, T, D]); x_r = sb("x_r", [P, T, D]); xT = sb("xT", [P, S])
        rope_c = sb("rope_c", [P, 2, S]); rope_s = sb("rope_s", [P, 2, S])
        qk = sb("qk", [P, 2, S]); rest = sb("rest", [P, 2, S])
        parts = sb("parts", [P, 3, 2, S], BF16)
        stack = sb("stack", [KM, 2, H, S], BF16)
        va = sb("va", [P, T, H, 32])
        negmax = sb("negmax", [P, H, T]); mrest = sb("mrest", [64, P])
        mparts = sb("mparts", [64, 3, P], BF16)
        probs = sb("probs", [P, PRING, S])
        ot = sb("ot", [P, GROUPS, S]); rden = sb("rden", [P, T, H]); on = sb("on", [P, T, D])
        onT = sb("onT", [P, S])
        r1 = sb("r1", [P, T, D]); stats = sb("stats", [P, T, 6]); mv = sb("mv", [P, T, 2])
        veps = sb("veps", [P, T]); rstd = sb("rstd", [P, T])
        x1 = sb("x1", [P, T, D]); x1T = sb("x1T", [P, S])
        logits = sb("logits", [P, T, E]); top = sb("top", [P, T, 8]); topi = sb("topi", [P, T, 8], U32)
        topf = sb("topf", [P, T, 2]); gap = sb("gap", [P, T]); egap = sb("egap", [P, T])
        den2 = sb("den2", [P, T]); rw = sb("rw", [P, T, 2])
        eq0 = sb("eq0", [P, T, E]); eq1 = sb("eq1", [P, T, E]); cw = sb("cw", [P, T, NE])
        th = sb("th", [P, 2, S]); gate = sb("gate", [P, 2, S]); hid = sb("hid", [P, 4, S])
        scaled = sb("scaled", [P, 2, T, D]); acc = sb("acc", [P, T, D])
        stats2 = sb("stats2", [P, T, 6]); mv2 = sb("mv2", [P, T, 2])
        veps2 = sb("veps2", [P, T]); rstd2 = sb("rstd2", [P, T])
        y_sb = sb("y_sb", [P, T, D])
        scratch = nc.dram_tensor("parts_scratch", [3, 2, P, S], BF16).ap()

        ps = ctx.enter_context(nc.psum_tensor("ps", [P, 8, S], F32))
        ATT, PV, G, U, Y = 0, 4, 5, 6, 7

        first_in = sem("first_in"); w_in = sem("w_in"); x_in = sem("x_in"); setup_v = sem("setup_v"); setup_p = sem("setup_p")
        xT_ps = sem("xT_ps"); xT_sb = sem("xT_sb"); qk_ps = sem("qk_ps"); v_ps = sem("v_ps")
        rope = sem("rope"); part0 = sem("part0"); part1 = sem("part1"); part2 = sem("part2")
        rest_done = sem("rest_done"); va_sb = sem("va_sb")
        scr_out = sem("scr_out"); stacked = sem("stacked")
        s_ps = sem("s_ps"); max_done = sem("max_done"); maxT_ps = sem("maxT_ps"); max_split = sem("max_split")
        max_in = sem("max_in")
        st_ps = sem("st_ps"); exp_done = sem("exp_done"); masked = sem("masked"); pv_ps = sem("pv_ps")
        ot_sb = sem("ot_sb"); oT_ps = sem("oT_ps"); on_sb = sem("on_sb"); onT_ps = sem("onT_ps")
        onT_sb = sem("onT_sb"); wo_ps = sem("wo_ps"); r1_done = sem("r1_done"); xr_in = sem("xr_in"); qk_sb = sem("qk_sb")
        var1 = sem("var1"); rstd1_done = sem("rstd1_done"); x1_sb = sem("x1_sb"); x1T_ps = sem("x1T_ps")
        x1T_sb = sem("x1T_sb"); logit_ps = sem("logit_ps"); gap_done = sem("gap_done"); egap_done = sem("egap_done")
        gu_ps = sem("gu_ps"); th_done = sem("th_done"); gate_done = sem("gate_done"); hid_done = sem("hid_done")
        y_ps = sem("y_ps"); scaled_done = sem("scaled_done"); acc_done = sem("acc_done")
        var2 = sem("var2"); rstd2_done = sem("rstd2_done"); y_sb_done = sem("y_sb_done"); out_done = sem("out_done")
        max_chain = sem("max_chain"); rden_done = sem("rden_done"); ln1_chain = sem("ln1_chain")
        route_chain = sem("route_chain"); ln2_chain = sem("ln2_chain"); logits_sb = sem("logits_sb")
        passed = sem("passed")

        block = ctx.enter_context(nc.Block())
        FIRST_LOADS, W_LOADS = 7, 11

        def first(b):
            return isinstance(b, int) and b == 0

        def carry(eng):
            eng.sem_inc(passed, 1)

        def each_sequence(eng, run):
            run(0, True, True, False)
            with eng.Fori(1, B - 1) as b:
                run(b, True, True, True)
            run(B - 1, True, False, True)
            run(B, False, False, True)

        @block.sync
        def _(sp):
            def load_x(b):
                if not first(b):
                    sp.wait_ge(xT_ps, b)
                    carry(sp)
                sp.dma_start(x_t[:, :, :], x[b].rearrange("(t p) d -> p t d", p=P)).then_inc(x_in, 16)

            def load_residual(b):
                if not first(b):
                    sp.wait_ge(r1_done, b)
                    carry(sp)
                sp.dma_start(x_r[:, :, :], x[b].rearrange("(t p) d -> p t d", p=P)).then_inc(xr_in, 16)

            def stack_parts(b):
                sp.wait_ge(part2, b + 1)
                carry(sp)
                sp.wait_ge(part1, b + 1)
                carry(sp)
                sp.dma_start(scratch.rearrange("a c p n -> p a c n"), parts[:, :, :, :]).then_inc(scr_out, 16)
                sp.wait_ge(scr_out, b * 16 + 16)
                carry(sp)
                if not first(b):
                    sp.wait_ge(st_ps, b * NB)
                    carry(sp)
                for s, both in enumerate(SLOTS):
                    for c, part in enumerate(both):
                        sp.dma_start(stack[DK * s:DK * s + DK, c, :, :],
                                     scratch[part, c].rearrange("(d h) n -> d h n", h=H)).then_inc(stacked, 16)

            sp.dma_start(ident_sb[:, :], ident).then_inc(first_in, 16)
            load_x(0)
            for dst, src in ((wq_sb, wq), (wk_sb, wk), (cos_sb, cos), (sin_sb, sin), (wv_sb, wv), (mask_f, mask)):
                sp.dma_start(dst[:, :], src).then_inc(first_in, 16)
            load_residual(0)
            sp.wait_ge(setup_v, 9)
            carry(sp)
            stack_parts(0)
            for dst, src in ((wo_sb, wo), (iota_sb, iota), (router_sb, router)):
                sp.dma_start(dst[:, :], src).then_inc(w_in, 16)
            sp.dma_start(bias_sb[:, :], bias.rearrange("(o e) -> o e", o=1).broadcast_to([P, E])).then_inc(w_in, 16)
            for dst, src, shared in ((w1_sb, w1, sw1), (w3_sb, w3, sw3)):
                sp.dma_start(dst[:, 0:E, :], src.rearrange("e d h -> d e h")).then_inc(w_in, 16)
                sp.dma_start(dst[:, E, :], shared[0]).then_inc(w_in, 16)
            for c in range(HALVES):
                sp.dma_start(w2_sb[:, 0:E, c, :], w2[:, c * P:(c + 1) * P, :].rearrange("e p d -> p e d")).then_inc(w_in, 16)
            sp.dma_start(w2_sb[:, E, :, :], sw2[0].rearrange("(c p) d -> p c d", p=P)).then_inc(w_in, 16)

            def run(b, attention, project_next, ffn):
                if attention:
                    if not isinstance(b, int) or b > 0:
                        load_residual(b)
                    if project_next:
                        load_x(b + 1)
                    sp.wait_ge(max_split, b + 1)
                    carry(sp)
                    for a in range(3):
                        sp.dma_start(stack[KZ + a:KZ + a + 1, 0, :, :].rearrange("o h (t q) -> o (h t) q", q=P),
                                     mparts[:, a, :]).then_inc(max_in, 16)
                if project_next:
                    stack_parts(b + 1)
                if ffn:
                    sp.wait_ge(y_sb_done, (b - 1) * T + T)
                    carry(sp)
                    sp.dma_start(out[b - 1].rearrange("(t p) d -> p t d", p=P), y_sb[:, :, :]).then_inc(out_done, 16)

            each_sequence(sp, run)
            sp.wait_ge(out_done, 16 * (B + 1))
            carry(sp)

        @block.gpsimd
        def _(pool):
            pool.memset(minus_half[:, :], -0.5).then_inc(setup_p, 1)
            pool.memset(va[:, :, :, :], 0.0).then_inc(setup_p, 1)
            pool.wait_ge(setup_p, 2)
            pool.memset(va[:, :, :, DK:DK + 1], 1.0).then_inc(setup_p, 1)
            pool.wait_ge(setup_p, 3)
            pool.memset(rstd[:, 0:1], 0.0).then_inc(scaled_done, 1)
            pool.memset(rstd[:, 1:2], 0.0).then_inc(out_done, 16)
            pool.memset(rstd[:, 2:3], 0.0).then_inc(acc_done, 1)
            pool.memset(rstd[:, 3:4], 0.0).then_inc(hid_done, 1)
            pool.memset(rstd2[:, 0:1], 0.0).then_inc(gate_done, 1)

            def mask_unit(b, v):
                pool.wait_ge(exp_done, b * NB + v + 1)
                carry(pool)
                blocks = PAIR_UNITS[v % NU]
                if len(blocks) == 2:
                    step = blocks[1][2]
                    area = probs[:, v % PRING, 0:step + P]
                    area = bass.AP(area.tensor, area.offset, [list(area.ap[0]), [step, 2], [1, P]])
                    pattern = [[0, 2], [1, P]]
                else:
                    area, pattern = probs[:, v % PRING, 0:P], [[1, P]]
                pool.affine_select(out=area, in_=area, compare_op=ALU.is_ge, fill=0.0, base=0,
                                   pattern=pattern, channel_multiplier=-1).then_inc(masked, 1)

            def add_expert(f, e):
                pool.wait_ge(scaled_done, f * NE + e + 2)
                pool.wait_ge(acc_done, f * NE + e + 1)
                pool.tensor_tensor(acc[:, :, :], x1[:, :, :] if e == 0 else acc[:, :, :],
                                   scaled[:, e % 2, :, :], ALU.add).then_inc(acc_done, 1)

            def run(b, attention, project_next, ffn):
                for kind, n in steps(attention, project_next, ffn):
                    if kind == "scores":
                        mask_unit(b, n)
                    elif kind == "scale":
                        add_expert(b - 1, n)
                    elif kind == "ln1":
                        pool.wait_ge(var1, b + 1)
                        pool.tensor_tensor(rstd[:, :], veps[:, :], minus_half[:, :], ALU.pow).then_inc(rstd1_done, 1)
                    elif kind == "ln2":
                        pool.wait_ge(var2, b)
                        pool.tensor_tensor(rstd2[:, :], veps2[:, :], minus_half[:, :], ALU.pow).then_inc(rstd2_done, 1)

            each_sequence(pool, run)

        @block.scalar
        def _(act):
            def exp_unit(b, v):
                act.wait_ge(st_ps, b * NB + v + 1)
                if v >= PRING:
                    act.wait_ge(pv_ps, b * GROUPS + (v - PRING) // UPG + 1)
                else:
                    if not first(b):
                        act.wait_ge(pv_ps, (b - 1) * GROUPS + (v + NB - PRING) // UPG + 1)
                act.activation(probs[:, v % PRING, :], ps[:, ATT + v % RING, :], ACT.Exp, scale=SCALE).then_inc(exp_done, 1)

            def project(b):
                act.wait_ge(xT_ps, b + 1)
                if not first(b):
                    act.wait_ge(v_ps, b)
                act.activation(xT[:, :], ps[:, ATT, :], ACT.Copy).then_inc(xT_sb, 1)

            def split_high(b):
                if not first(b):
                    act.wait_ge(scr_out, b * 16)
                act.wait_ge(qk_sb, b + 1)
                act.activation(parts[:, 0, :, :], qk[:, :, :], ACT.Copy).then_inc(part0, 1)

            def split_mid(b):
                act.wait_ge(rest_done, b + 1)
                act.activation(parts[:, 1, :, :], rest[:, :, :], ACT.Copy).then_inc(part1, 1)

            def store_v(b):
                if not first(b):
                    act.wait_ge(pv_ps, b * GROUPS)
                act.wait_ge(v_ps, b + 1)
                act.activation(va[:, :, :, 0:DK], ps[:, PV, :].rearrange("p (t h d) -> p t h d", t=T, h=H),
                               ACT.Copy).then_inc(va_sb, 1)

            def run(b, attention, project_next, ffn):
                f = b - 1
                for kind, n in steps(attention, project_next, ffn):
                    if kind == "scores":
                        exp_unit(b, n)
                    elif kind == "x_T":
                        project(b + 1)
                    elif kind == "rope":
                        split_high(b + 1)
                    elif kind == "rest":
                        split_mid(b + 1)
                    elif kind == "v":
                        store_v(b + 1)
                    elif kind == "out":
                        act.wait_ge(onT_ps, b + 1)
                        act.activation(onT[:, :], ps[:, PV, :], ACT.Copy).then_inc(onT_sb, 1)
                    elif kind == "x1_T":
                        act.wait_ge(x1T_ps, b)
                        act.activation(x1T[:, :], ps[:, PV, :], ACT.Copy).then_inc(x1T_sb, 1)
                    elif kind == "router":
                        act.wait_ge(gap_done, b)
                        act.activation(egap[:, :], gap[:, :], ACT.Exp).then_inc(egap_done, 1)
                    elif kind == "tanh":
                        act.wait_ge(gu_ps, f * CH + n + 1)
                        if n >= 2:
                            act.wait_ge(gate_done, f * CH + n)
                        act.activation(th[:, n % 2, :], ps[:, G, :], ACT.Tanh, scale=0.5).then_inc(th_done, 1)

            act.wait_ge(setup_p, 3)
            project(0)
            store_v(0)
            split_high(0)
            split_mid(0)
            each_sequence(act, run)

        @block.tensor
        def _(pe):
            def x_transposes(b):
                pe.wait_ge(x_in, b * 16 + 16)
                if not first(b):
                    pe.wait_ge(max_done, b * NA)
                for t in range(T):
                    last = pe.transpose(ps[:, ATT, t * P:(t + 1) * P], x_t[:, t, :], ident_sb[:, :])
                last.then_inc(xT_ps, 1)

            def project(b):
                pe.wait_ge(xT_sb, b + 1)
                for n, w in enumerate((wq_sb, wk_sb, wqr_sb, wkr_sb)):
                    last = pe.matmul(ps[:, ATT + n, :], w[:, :], xT[:, :], start=True, stop=True)
                last.then_inc(qk_ps, 1)

            def project_v(b):
                if not first(b):
                    pe.wait_ge(ot_sb, b * GROUPS)
                for t in range(T):
                    last = pe.matmul(ps[:, PV, t * P:(t + 1) * P], xT[:, t * P:(t + 1) * P], wv_sb[:, :],
                                     start=True, stop=True)
                last.then_inc(v_ps, 1)

            def max_unit(b, u):
                i, h0, n, stride = MAX_UNITS[u]
                if u == 0:
                    if not first(b):
                        pe.wait_ge(exp_done, b * NB)
                    pe.wait_ge(stacked, b * (32 * len(SLOTS)) + 32 * len(SLOTS))
                    if not first(b):
                        pe.wait_ge(r1_done, b)
                if u >= RING:
                    pe.wait_ge(max_done, b * NA + u - RING + 1)
                unit = ps[:, ATT + u % RING, :]
                for k in range(n):
                    at = k * stride
                    w = (i + 1) * P
                    pe.matmul(unit[:, at:at + w], stack[0:KZ, 0, h0 + k, i * P:(i + 1) * P],
                              stack[0:KZ, 1, h0 + k, 0:w], start=True, stop=False)
                    last = pe.matmul(unit[:, at + w - P:at + w], ident_bf[:, :], mask_bf[:, :],
                                     start=False, stop=True)
                last.then_inc(s_ps, 1)

            def max_rows(b):
                pe.wait_ge(max_done, b * NA + NA)
                pe.wait_ge(va_sb, b + 1)
                carry(pe)
                pe.transpose(ps[0:H * T, PV, 0:P], negmax[:, :, :].rearrange("p h t -> p (h t)"), ident_sb[:, :])\
                  .then_inc(maxT_ps, 1)

            def scores_unit(b, v, project_next):
                if v == 0:
                    pe.wait_ge(max_in, b * 48 + 48)
                    if project_next:
                        pe.wait_ge(rope, b + 2)
                if v >= RING:
                    pe.wait_ge(exp_done, b * NB + v - RING + 1)
                unit = ps[:, ATT + v % RING, :]
                for k, j, at in PAIR_UNITS[v % NU]:
                    h = 2 * (v // NU) + k
                    last = pe.matmul(unit[:, at:at + S - j * P], stack[0:KM, 1, h, j * P:(j + 1) * P],
                                     stack[0:KM, 0, h, j * P:S], start=True, stop=True)
                last.then_inc(st_ps, 1)

            def weighted_values(b, g):
                pe.wait_ge(masked, b * NB + UPG * (g + 1))
                if g >= 1:
                    pe.wait_ge(ot_sb, b * GROUPS + g)
                for j in range(T):
                    for k in range(PER_PV):
                        n, at = next((n, at) for n, unit in enumerate(PAIR_UNITS)
                                     for kk, jj, at in unit if (kk, jj) == (k % 2, j))
                        v = UPG * g + NU * (k // 2) + n
                        last = pe.matmul(ps[32 * k:32 * k + 32, PV, j * P:S], va[:, j, PER_PV * g + k, :],
                                         probs[:, v % PRING, at:at + S - j * P], start=(j == 0), stop=(j == T - 1),
                                         skip_group_check=True)
                last.then_inc(pv_ps, 1)

            def heads_transposes(b, project_next):
                pe.wait_ge(ot_sb, b * GROUPS + GROUPS)
                pe.wait_ge(exp_done, b * NB + NB)
                for t in range(T):
                    for g in range(GROUPS):
                        last = pe.transpose(ps[:, ATT + t, g * P:(g + 1) * P], ot[:, g, t * P:(t + 1) * P], ident_sb[:, :])
                    last.then_inc(oT_ps, 1)

            def out_transposes(b, project_next):
                if project_next:
                    pe.wait_ge(va_sb, b + 2)
                for t in range(T):
                    pe.wait_ge(on_sb, b * T + t + 1)
                    last = pe.transpose(ps[:, PV, t * P:(t + 1) * P], on[:, t, :], ident_sb[:, :])
                last.then_inc(onT_ps, 1)

            def project_out(b):
                pe.wait_ge(onT_sb, b + 1)
                for t in range(T):
                    last = pe.matmul(ps[:, ATT, t * P:(t + 1) * P], onT[:, t * P:(t + 1) * P], wo_sb[:, :],
                                     start=True, stop=True)
                last.then_inc(wo_ps, 1)

            def x1_transposes(f):
                for t in range(T):
                    pe.wait_ge(x1_sb, f * T + t + 1)
                    last = pe.transpose(ps[:, PV, t * P:(t + 1) * P], x1[:, t, :], ident_sb[:, :])
                last.then_inc(x1T_ps, 1)

            def route(f):
                pe.wait_ge(x1T_sb, f + 1)
                pe.wait_ge(scaled_done, f * NE + 1)
                for t in range(T):
                    last = pe.matmul(ps[:, Y, t * E:(t + 1) * E], x1T[:, t * P:(t + 1) * P], router_sb[:, :],
                                     start=True, stop=True)
                last.then_inc(logit_ps, 1)

            def up(f, c):
                e, half = c // HALVES, c % HALVES
                for bank, w, free in ((G, w1_sb, gate_done), (U, w3_sb, hid_done)):
                    pe.wait_ge(free, f * CH + c + 1)
                    last = pe.matmul(ps[:, bank, :], w[:, e, half * P:(half + 1) * P], x1T[:, :], start=True, stop=True)
                last.then_inc(gu_ps, 1)

            def down(f, e):
                pe.wait_ge(hid_done, f * CH + HALVES * (e + 1) + 1)
                if e == 0:
                    pe.wait_ge(logits_sb, f + 1)
                else:
                    pe.wait_ge(scaled_done, f * NE + e + 1)
                for t in range(T):
                    for half in range(HALVES):
                        c = e * HALVES + half
                        last = pe.matmul(ps[:, Y, t * P:(t + 1) * P], hid[:, c % 4, t * P:(t + 1) * P],
                                         w2_sb[:, e, half, :], start=(half == 0), stop=(half == HALVES - 1))
                last.then_inc(y_ps, 1)

            def run(b, attention, project_next, ffn):
                f = b - 1
                for kind, n in steps(attention, project_next, ffn):
                    if kind == "max":
                        max_unit(b, n)
                    elif kind == "max_rows":
                        max_rows(b)
                    elif kind == "scores":
                        scores_unit(b, n, project_next)
                    elif kind == "values":
                        weighted_values(b, n)
                    elif kind == "x_T":
                        x_transposes(b + 1)
                    elif kind == "project":
                        project(b + 1)
                    elif kind == "v":
                        project_v(b + 1)
                    elif kind == "heads_T":
                        heads_transposes(b, project_next)
                    elif kind == "out_T":
                        out_transposes(b, project_next)
                    elif kind == "out":
                        project_out(b)
                    elif kind == "x1_T":
                        x1_transposes(f)
                    elif kind == "router":
                        route(f)
                    elif kind == "up":
                        up(f, n)
                    elif kind == "down":
                        down(f, n)

            pe.wait_ge(first_in, 16 * FIRST_LOADS)
            pe.wait_ge(setup_v, 9)
            pe.wait_ge(setup_p, 3)
            x_transposes(0)
            project(0)
            project_v(0)
            pe.wait_ge(w_in, 16 * W_LOADS)
            each_sequence(pe, run)

        @block.vector
        def _(dve):
            dve.wait_ge(first_in, 16 * FIRST_LOADS)
            for src, dst in ((wq_sb, wqr_sb), (wk_sb, wkr_sb)):
                s4 = src[:, :].rearrange("p (a e h) -> p a e h", e=2, h=H)
                d4 = dst[:, :].rearrange("p (a e h) -> p a e h", e=2, h=H)
                dve.tensor_scalar(d4[:, :, 0, :], s4[:, :, 1, :], -1.0, None, ALU.mult).then_inc(setup_v, 1)
                dve.tensor_copy(d4[:, :, 1, :], s4[:, :, 0, :]).then_inc(setup_v, 1)
            dve.tensor_copy(ident_bf[:, :], ident_sb[:, :]).then_inc(setup_v, 1)
            dve.tensor_copy(mask_bf[:, :], mask_f[:, :]).then_inc(setup_v, 1)
            dve.memset(stack[KZ:KM, 1, :, :], 1.0).then_inc(setup_v, 1)
            dve.memset(stack[32:64, :, :, :], 0.0).then_inc(setup_v, 1)
            dve.memset(stack[64:KZ, :, :, :], 0.0).then_inc(setup_v, 1)

            def link(ins, semaphore, value):
                ins.then_inc(semaphore, 1)
                dve.wait_ge(semaphore, value)

            def rope_qk(b):
                dve.wait_ge(qk_ps, b + 1)
                for dst, bank, table in ((rope_c, ATT, cos_sb), (rope_s, ATT + 2, sin_sb)):
                    ins = dve.tensor_tensor(dst[:, :, :], ps[:, bank:bank + 2, :],
                                            table[:, :].rearrange("p (o n) -> p o n", o=1).broadcast_to([P, 2, S]), ALU.mult)
                link(ins, rope, b + 1)
                dve.tensor_tensor(qk[:, :, :], rope_c[:, :, :], rope_s[:, :, :], ALU.add).then_inc(qk_sb, 1)

            def split_rest(b):
                dve.wait_ge(part0, b + 1)
                dve.tensor_tensor(rest[:, :, :], qk[:, :, :], parts[:, 0, :, :], ALU.subtract).then_inc(rest_done, 1)

            def split_low(b):
                dve.wait_ge(part1, b + 1)
                dve.tensor_tensor(parts[:, 2, :, :], rest[:, :, :], parts[:, 1, :, :], ALU.subtract).then_inc(part2, 1)

            def max_unit(b, u):
                i, h0, n, stride = MAX_UNITS[u]
                dve.wait_ge(s_ps, b * NA + u + 1)
                unit = ps[:, ATT + u % RING, :].rearrange("p (h s) -> p h s", s=stride)
                dve.tensor_reduce(negmax[:, h0:h0 + n, i], unit[:, :, 0:(i + 1) * P], AX_X, ALU.max,
                                  negate=True).then_inc(max_done, 1)

            def split_max(b):
                dve.wait_ge(maxT_ps, b + 1)
                mT = ps[0:H * T, PV, 0:P]
                link(dve.tensor_copy(mparts[:, 0, :], mT), max_chain, 3 * b + 1)
                link(dve.tensor_tensor(mrest[:, :], mT, mparts[:, 0, :], ALU.subtract), max_chain, 3 * b + 2)
                link(dve.tensor_copy(mparts[:, 1, :], mrest[:, :]), max_chain, 3 * b + 3)
                dve.tensor_tensor(mparts[:, 2, :], mrest[:, :], mparts[:, 1, :], ALU.subtract).then_inc(max_split, 1)

            def values_out(b, g):
                dve.wait_ge(pv_ps, b * GROUPS + g + 1)
                dve.tensor_copy(ot[:, g, :], ps[:, PV, :]).then_inc(ot_sb, 1)

            def normalize(b):
                for t in range(T):
                    dve.wait_ge(oT_ps, b * T + t + 1)
                    oq = ps[:, ATT + t, :].rearrange("p (h c) -> p h c", c=32)
                    ins = dve.reciprocal(rden[:, t, :], oq[:, :, DK])
                link(ins, rden_done, b + 1)
                for t in range(T):
                    oq = ps[:, ATT + t, :].rearrange("p (h c) -> p h c", c=32)
                    dve.tensor_tensor(on[:, t, :].rearrange("p (h d) -> p h d", d=DK), oq[:, :, 0:DK],
                                      rden[:, t, :].rearrange("p (h o) -> p h o", o=1).broadcast_to([P, H, DK]),
                                      ALU.mult).then_inc(on_sb, 1)

            def layernorm_stats(b, src, st, m, ve, chain, var_sem):
                for t in range(T):
                    ins = dve.bn_stats(st[:, t, :], src[:, t, :])
                link(ins, chain, 2 * b + 1)
                carry(dve)
                for t in range(T):
                    ins = dve.bn_aggr(m[:, t, :], st[:, t, :])
                link(ins, chain, 2 * b + 2)
                dve.tensor_scalar(ve[:, :], m[:, :, 1], EPS, None, ALU.add).then_inc(var_sem, 1)

            def layernorm_end(b, src, m, rs, rstd_sem, dst, dst_sem):
                dve.wait_ge(rstd_sem, b + 1)
                for t in range(T):
                    dve.tensor_scalar(dst[:, t, :], src[:, t, :], m[:, t, 0:1], rs[:, t:t + 1],
                                      ALU.subtract, ALU.mult).then_inc(dst_sem, 1)

            def layernorm1_stats(b):
                dve.wait_ge(wo_ps, b + 1)
                dve.wait_ge(xr_in, b * 16 + 16)
                link(dve.tensor_tensor(r1[:, :, :], x_r[:, :, :], ps[:, ATT, :].rearrange("p (t d) -> p t d", t=T), ALU.add),
                     r1_done, b + 1)
                layernorm_stats(b, r1, stats, mv, veps, ln1_chain, var1)

            def layernorm1_end(b, ffn):
                if ffn:
                    dve.wait_ge(acc_done, (b - 1) * NE + 2)
                layernorm_end(b, r1, mv, rstd, rstd1_done, x1, x1_sb)

            def route(f):
                step = [ROUTE * f]

                def step_on(ins):
                    step[0] = step[0] + 1
                    link(ins, route_chain, step[0])

                dve.wait_ge(logit_ps, f + 1)
                link(dve.tensor_tensor(logits[:, :, :], ps[:, Y, 0:T * E].rearrange("p (t e) -> p t e", t=T),
                                       bias_sb[:, :].rearrange("p (o e) -> p o e", o=1).broadcast_to([P, T, E]), ALU.add),
                     logits_sb, f + 1)
                carry(dve)
                for t in range(T):
                    ins = dve.max(top[:, t, :], logits[:, t, :])
                step_on(ins)
                carry(dve)
                for t in range(T):
                    ins = dve.max_index(topi[:, t, :], top[:, t, :], logits[:, t, :])
                dve.tensor_tensor(gap[:, :], top[:, :, 1], top[:, :, 0], ALU.subtract).then_inc(gap_done, 1)
                step_on(ins)
                step_on(dve.tensor_copy(topf[:, :, :], topi[:, :, 0:2]))
                dve.wait_ge(egap_done, f + 1)
                step_on(dve.tensor_scalar(den2[:, :], egap[:, :], 2.0, 2.0, ALU.mult, ALU.add))
                step_on(dve.reciprocal(rw[:, :, 0], den2[:, :]))
                step_on(dve.tensor_tensor(rw[:, :, 1], rw[:, :, 0], egap[:, :], ALU.mult))
                for n, eq in enumerate((eq0, eq1)):
                    ins = dve.tensor_tensor(eq[:, :, :], iota_sb[:, :].rearrange("p (o e) -> p o e", o=1).broadcast_to([P, T, E]),
                                            topf[:, :, n:n + 1].broadcast_to([P, T, E]), ALU.is_equal)
                step_on(ins)
                for n, eq in enumerate((eq0, eq1)):
                    ins = dve.tensor_tensor(eq[:, :, :], eq[:, :, :], rw[:, :, n:n + 1].broadcast_to([P, T, E]), ALU.mult)
                step_on(ins)
                dve.tensor_tensor(cw[:, :, 0:E], eq0[:, :, :], eq1[:, :, :], ALU.add)
                step_on(dve.memset(cw[:, :, E:NE], 0.5))

            ROUTE = 9

            def gated(f, c):
                dve.wait_ge(th_done, f * CH + c + 1)
                link(dve.scalar_tensor_tensor(out=gate[:, c % 2, :], in0=th[:, c % 2, :], scalar=1.0, in1=ps[:, G, :],
                                              op0=ALU.add, op1=ALU.mult), gate_done, f * CH + c + 2)
                if c >= 4:
                    dve.wait_ge(y_ps, f * NE + (c - 4) // HALVES + 1)
                dve.tensor_tensor(hid[:, c % 4, :], gate[:, c % 2, :], ps[:, U, :], ALU.mult).then_inc(hid_done, 1)

            def scale_expert(f, e):
                dve.wait_ge(y_ps, f * NE + e + 1)
                if e >= 2:
                    dve.wait_ge(acc_done, f * NE + e)
                dve.tensor_tensor(scaled[:, e % 2, :, :], ps[:, Y, :].rearrange("p (t d) -> p t d", t=T),
                                  cw[:, :, e:e + 1].broadcast_to([P, T, D]), ALU.mult).then_inc(scaled_done, 1)

            def layernorm2_stats(f):
                dve.wait_ge(acc_done, f * NE + NE + 1)
                layernorm_stats(f, acc, stats2, mv2, veps2, ln2_chain, var2)

            def layernorm2_end(f):
                dve.wait_ge(out_done, f * 16 + 16)
                layernorm_end(f, acc, mv2, rstd2, rstd2_done, y_sb, y_sb_done)

            def run(b, attention, project_next, ffn):
                f = b - 1
                for kind, n in steps(attention, project_next, ffn):
                    if kind == "max":
                        max_unit(b, n)
                    elif kind == "max_rows":
                        split_max(b)
                    elif kind == "values":
                        values_out(b, n)
                    elif kind == "rope":
                        rope_qk(b + 1)
                    elif kind == "rest":
                        split_rest(b + 1)
                    elif kind == "low":
                        split_low(b + 1)
                    elif kind == "norm":
                        normalize(b)
                    elif kind == "ln1_stats":
                        layernorm1_stats(b)
                    elif kind == "ln1":
                        layernorm1_end(b, ffn)
                    elif kind == "router":
                        route(f)
                    elif kind == "glu":
                        gated(f, n)
                    elif kind == "scale":
                        scale_expert(f, n)
                    elif kind == "ln2_stats":
                        layernorm2_stats(f)
                    elif kind == "ln2":
                        layernorm2_end(f)

            rope_qk(0)
            split_rest(0)
            split_low(0)
            dve.wait_ge(w_in, 16 * W_LOADS)
            each_sequence(dve, run)


_INS = ["x", "wq", "wk", "wv", "wo", "cos", "sin", "ident", "mask", "iota", "router", "bias",
        "w1", "w3", "w2", "sw1", "sw3", "sw2"]


def kernel(L0_attn_x, L0_attn_Wq, L0_attn_Wk, L0_attn_Wv, L0_attn_Wo, L0_ffn_router_w, L0_ffn_experts_bias,
           L0_ffn_w1, L0_ffn_w3, L0_ffn_w2, L0_ffn_sw1, L0_ffn_sw3, L0_ffn_sw2):
    import numpy as np
    import concourse.bacc as bacc
    from concourse.bass_utils import run_bass_kernel_spmd

    B, S, D = L0_attn_x.shape
    H, E = 16, L0_ffn_w1.shape[0]
    dk = D // H
    inv_freq = (1.0 / 10000.0 ** (np.arange(0, dk, 2, dtype=np.float32) / np.float32(dk))).astype(np.float32)
    angles = np.outer(np.arange(S, dtype=np.float32), inv_freq).astype(np.float32)
    table = lambda f: np.repeat(np.repeat(f(angles).astype(np.float32), 2, axis=1).T, H, axis=0)
    by_dim = lambda w: np.asarray(w).reshape(D, H, dk).transpose(0, 2, 1).reshape(D, D)
    arrays = {
        "x": L0_attn_x, "wq": by_dim(L0_attn_Wq), "wk": by_dim(L0_attn_Wk), "wv": L0_attn_Wv, "wo": L0_attn_Wo,
        "cos": table(np.cos), "sin": table(np.sin), "ident": np.eye(P, dtype=np.float32),
        "mask": np.triu(np.full((P, P), NEG, np.float32), 1),
        "iota": np.tile(np.arange(E, dtype=np.float32), (P, 1)),
        "router": np.asarray(L0_ffn_router_w).T, "bias": L0_ffn_experts_bias,
        "w1": L0_ffn_w1, "w3": L0_ffn_w3, "w2": L0_ffn_w2, "sw1": L0_ffn_sw1, "sw3": L0_ffn_sw3, "sw2": L0_ffn_sw2,
    }
    arrays = {f"in_{k}": np.ascontiguousarray(v) for k, v in arrays.items()}
    nc = bacc.Bacc("TRN2", target_bir_lowering=False, num_devices=1)
    args = [nc.dram_tensor(f"in_{k}", arrays[f"in_{k}"].shape, mybir.dt.from_np(arrays[f"in_{k}"].dtype),
                           kind="ExternalInput").ap() for k in _INS]
    out = nc.dram_tensor("out", (B, S, D), F32, kind="ExternalOutput").ap()
    build_block(nc, *args, out)
    r = run_bass_kernel_spmd(nc, [arrays], core_ids=[0])
    return r.results[0]["out"]
```

```python
from contextlib import ExitStack

import concourse.bass as bass
from concourse import mybir

ALU = mybir.AluOpType
ACT = mybir.ActivationFunctionType
F32 = mybir.dt.float32
BF16 = mybir.dt.bfloat16
F32R = mybir.dt.float32r
U32 = mybir.dt.uint32
AX_X = mybir.AxisListType.X

P = 128
NEG = -3.0e38
EPS = 1e-5
SLOTS = [(0, 0), (0, 1), (1, 0), (1, 1), (0, 2), (2, 0)]


VALUES_AT, V_AT = 2.51, 3.53
PREVIOUS = [(3.03, "heads_T", 0), (4.64, "norm", 0), (5.05, "heads_T", 1), (5.57, "norm", 1), (7.66, "out_T", 0),
            (8.42, "out", 0), (7.97, "ln1_stats", 0), (8.57, "ln1", 0), (9.32, "x1_T", 0),
            (9.16, "x1_split", 0), (11.45, "router", 0), (12.18, "weights", 0)]
NEXT = [(5.04, "x_T", 0), (6.01, "project", 0), (6.95, "project", 1), (8.45, "rope", 0), (10.6, "rest", 0),
        (11.92, "low", 0)]
MAX_AT = [(24.28, 36.36, 37.18), (7.0, 16.32, 16.98)]
UP_AT = (9.66, 22.15, 35.12, 47.0)
LAST_DOWN = 1.98
LAGS = (0.05, 0.05, 0.05, 1.16, 0.96)


def build_block(nc, x, wq, wk, wv, wo, cos, sin, ident, mask, iota, router, bias,
                w1, w3, w2, sw1, sw3, sw2, out):
    B, S, D = x.shape
    E, _, HID = w1.shape
    H = 16
    DK = D // H
    T = S // P
    SCALE = float(DK) ** -0.5
    HALVES = HID // P
    NE = E + 1
    CH = NE * HALVES
    KS = DK * len(SLOTS)
    KZ = 96
    KM = KZ + 3
    PER_PV = 4

    HH = H // 2
    MAX_UNITS = []
    for half in range(2):
        for i in range(T):
            stride = {0: 128, 1: 256, 2: 512, 3: 512}[i]
            n = S // stride
            MAX_UNITS += [(i, half * HH + h, n, stride) for h in range(0, HH, n)]
    NA = len(MAX_UNITS)
    NAH = NA // 2
    PAIRS = H // 2
    PAIR_UNITS = [[(0, 1, 0), (0, 3, 3 * P)], [(0, 0, 0)], [(1, 1, 0), (1, 3, 3 * P)], [(1, 0, 0)],
                  [(0, 2, 0), (1, 2, 2 * P)]]
    NU = len(PAIR_UNITS)
    NB = NU * PAIRS
    GROUPS = H // PER_PV
    UPG = NB // GROUPS
    PRING = 2 * UPG

    def first(s):
        return isinstance(s, int) and s == 0

    def last_one(s):
        return isinstance(s, int) and s == B - 1

    MU = T + 4 + NA
    assert MU % 2 == 0 and NAH % 2 == 0 and T % 2 == 0

    def project_use(s, n):
        return n if first(s) else PASS0 + MU * (s - 1) + T + n

    def max_use(s, u):
        if u < NAH:
            return 4 + u if first(s) else PASS0 + MU * (s - 1) + T + 4 + NAH + u
        return PASS0 + MU * s + T + (0 if last_one(s) else 4) + u - NAH

    def heads_use(s, t):
        return (PASS0 + MU * s + T + NAH if last_one(s) else PASS0 + MU * (s + 1)) + t

    PASS0 = 4 + NAH - T

    def steps(b):
        here = lambda lag: not isinstance(b, int) or 0 <= b - lag < B
        events = []

        def add(at, kind, n, lag):
            events.append((at, len(events), kind, n, lag))

        for v in range(NB):
            add(v, "scores", v, 0)
        for g in range(GROUPS - 1):
            add(VALUES_AT + UPG * (g + 1), "values", g, 0)
        add(VALUES_AT, "values", GROUPS - 1, 1)
        for at, kind, n in PREVIOUS:
            add(at, kind, n, 1)
        add(V_AT, "v", 0, 0)
        for at, kind, n in NEXT:
            add(at, kind, n, -1)
        for half, (begin, end, rows) in enumerate(MAX_AT):
            for k in range(NAH):
                add(begin + (end - begin) * k / (NAH - 1), "max", NAH * half + k, half - 1 if half == 0 else 0)
            add(rows, "max_rows", half, half - 1 if half == 0 else 0)
        for c in range(CH):
            k = min(int(c / (CH - 1) * (len(UP_AT) - 1)), len(UP_AT) - 2)
            at = UP_AT[k] + (UP_AT[k + 1] - UP_AT[k]) * (c / (CH - 1) * (len(UP_AT) - 1) - k)
            e = c // HALVES
            experts = [(0, "gate", c), (LAGS[0], "tanh", c), (LAGS[1], "up", c), (LAGS[2], "glu", c)]
            if c % HALVES == HALVES - 1:
                experts += [(LAGS[3], "down", e), (LAGS[4], "scale", e)]
            if c == CH - 1:
                experts += [(LAGS[4] + 0.5, "ln2_stats", 0), (LAGS[4] + 1.0, "ln2", 0)]
            for behind, kind, n in experts:
                lag = 1 + int((at + behind) // NB)
                alone = LAST_DOWN if last_one(b - lag) and kind in ("down", "scale") and c < CH - 1 else 0
                add((at + behind) % NB + alone, kind, n, lag)
        return [(kind, n, lag) for _, _, kind, n, lag in sorted(events) if here(lag)]

    with ExitStack() as ctx:
        def sb(name, shape, dt=F32):
            return ctx.enter_context(nc.sbuf_tensor(name, shape, dt))

        def sem(name):
            return ctx.enter_context(nc.semaphore(name))

        wq_sb = sb("wq_sb", [P, D]); wk_sb = sb("wk_sb", [P, D]); wv_sb = sb("wv_sb", [P, D])
        wo_sb = sb("wo_sb", [P, D])
        wqr_sb = sb("wqr_sb", [P, D]); wkr_sb = sb("wkr_sb", [P, D])
        cos_sb = sb("cos_sb", [P, S]); sin_sb = sb("sin_sb", [P, S])
        ident_sb = sb("ident_sb", [P, P]); mask_f = sb("mask_f", [P, P])
        ident_bf = sb("ident_bf", [P, P], BF16); mask_bf = sb("mask_bf", [P, P], BF16)
        iota_sb = sb("iota_sb", [P, E]); bias_sb = sb("bias_sb", [P, E]); router_sb = sb("router_sb", [P, E])
        w1_hi = sb("w1_hi", [P, NE, HID], F32R); w1_lo = sb("w1_lo", [P, NE, HID], F32R)
        w3_hi = sb("w3_hi", [P, NE, HID], F32R); w3_lo = sb("w3_lo", [P, NE, HID], F32R)
        w2_sb = sb("w2_sb", [P, NE, HALVES, D])
        minus_half = sb("minus_half", [P, T])
        x_t = sb("x_t", [P, T, D]); x_r = sb("x_r", [P, T, D]); xT = sb("xT", [P, S])
        qk = sb("qk", [P, 2, S]); rest = sb("rest", [P, 2, S])
        parts = sb("parts", [P, 3, 2, S], BF16)
        stack = sb("stack", [KM, 2, H, S], BF16)
        va = sb("va", [P, T, H, 32])
        negmax = sb("negmax", [P, H, T]); mrest = sb("mrest", [HH * T, P])
        mparts = sb("mparts", [HH * T, 3, P], BF16)
        probs = sb("probs", [P, PRING, S])
        ot = sb("ot", [P, GROUPS, S]); rden = sb("rden", [P, T, H]); on = sb("on", [P, T, D])
        onT = sb("onT", [P, S])
        r1 = sb("r1", [P, T, D]); stats = sb("stats", [P, T, 6]); mv = sb("mv", [P, T, 2])
        veps = sb("veps", [P, T]); rstd = sb("rstd", [P, T])
        x1 = sb("x1", [P, T, D]); x1T = sb("x1T", [P, S])
        x1T_hi = sb("x1T_hi", [P, S], F32R); x1T_lo = sb("x1T_lo", [P, S], F32R)
        logits = sb("logits", [P, T, E]); top = sb("top", [P, T, 8]); topi = sb("topi", [P, T, 8], U32)
        topf = sb("topf", [P, T, 2]); gap = sb("gap", [P, T]); egap = sb("egap", [P, T])
        den2 = sb("den2", [P, T]); rw = sb("rw", [P, T, 2])
        eq0 = sb("eq0", [P, T, E]); eq1 = sb("eq1", [P, T, E]); cw = sb("cw", [P, T, NE])
        th = sb("th", [P, 2, S]); gate = sb("gate", [P, 2, S]); hid = sb("hid", [P, 4, S])
        scaled = sb("scaled", [P, 2, T, D]); acc = sb("acc", [P, T, D])
        stats2 = sb("stats2", [P, T, 6]); mv2 = sb("mv2", [P, T, 2])
        veps2 = sb("veps2", [P, T]); rstd2 = sb("rstd2", [P, T])
        y_sb = sb("y_sb", [P, T, D])
        scratch = nc.dram_tensor("parts_scratch", [3, 2, P, S], BF16).ap()

        ps = ctx.enter_context(nc.psum_tensor("ps", [P, 8, S], F32))
        SC, M, PV, G, Y = 0, 2, 4, 5, 7

        ident_in = sem("ident_in"); qk_in = sem("qk_in"); first_in = sem("first_in"); w_in = sem("w_in"); x_in = sem("x_in"); setup_v = sem("setup_v"); setup_p = sem("setup_p")
        xT_ps = sem("xT_ps"); xT_sb = sem("xT_sb"); v_ps = sem("v_ps")
        part0 = sem("part0"); part1 = sem("part1"); part2 = sem("part2")
        rest_done = sem("rest_done"); va_sb = sem("va_sb")
        scr_out = sem("scr_out"); stacked = [sem("stacked_first_half"), sem("stacked_second_half")]
        m_filled = sem("m_filled"); m_used = sem("m_used"); maxT_ps = sem("maxT_ps"); max_split = sem("max_split")
        max_in = sem("max_in")
        st_ps = sem("st_ps"); exp_done = sem("exp_done"); masked = sem("masked"); pv_ps = sem("pv_ps")
        ot_sb = sem("ot_sb"); onT_ps = sem("onT_ps")
        onT_sb = sem("onT_sb"); wo_ps = sem("wo_ps"); r1_done = sem("r1_done"); xr_in = sem("xr_in"); qk_sb = sem("qk_sb")
        var1 = sem("var1"); rstd1_done = sem("rstd1_done"); x1_sb = sem("x1_sb"); x1T_ps = sem("x1T_ps")
        x1T_sb = sem("x1T_sb"); logit_ps = sem("logit_ps"); gap_done = sem("gap_done"); egap_done = sem("egap_done")
        w_hi = sem("w_hi"); w_lo = sem("w_lo"); x1T_high = sem("x1T_high"); x1T_low = sem("x1T_low")
        g_ps = sem("g_ps"); u_ps = sem("u_ps"); th_done = sem("th_done"); gate_done = sem("gate_done"); hid_done = sem("hid_done")
        y_ps = sem("y_ps"); scaled_done = sem("scaled_done"); acc_done = sem("acc_done")
        var2 = sem("var2"); rstd2_done = sem("rstd2_done"); y_sb_done = sem("y_sb_done"); out_done = sem("out_done")
        max_chain = sem("max_chain"); rden_done = sem("rden_done"); ln1_chain = sem("ln1_chain")
        route_chain = sem("route_chain"); ln2_chain = sem("ln2_chain"); logits_sb = sem("logits_sb")
        passed = sem("passed")

        def room(tile, n):
            return tile.rearrange("p a s -> p (a s)")[:, 0:n * HID].rearrange("p (e h) -> p e h", h=HID)

        def some(w, e0, e1):
            return w[e0:e1].rearrange("e d h -> d e h")

        half_e = E // 2
        staged = [(room(hid[:, :, :], E), w1_hi[:, 0:E, :], w1_lo[:, 0:E, :], some(w1, 0, E)),
                  (room(th[:, :, :], half_e), w3_hi[:, 0:half_e, :], w3_lo[:, 0:half_e, :], some(w3, 0, half_e)),
                  (room(gate[:, :, :], half_e), w3_hi[:, half_e:E, :], w3_lo[:, half_e:E, :], some(w3, half_e, E)),
                  (room(acc[:, :, :], 1), w1_hi[:, E:NE, :], w1_lo[:, E:NE, :], some(sw1, 0, 1)),
                  (room(x1[:, :, :], 1), w3_hi[:, E:NE, :], w3_lo[:, E:NE, :], some(sw3, 0, 1))]

        block = ctx.enter_context(nc.Block())
        STACK = 16 * 2 * len(SLOTS)
        FIRST_LOADS, W_LOADS = 6, 10

        def carry(eng):
            eng.sem_inc(passed, 1)

        def two_banks(f):
            return last_one(f)

        def gate_bank(f, c):
            return SC if two_banks(f) and c % 2 == 1 else G

        def later_passes(eng, run):
            run(1)
            with eng.Fori(2, B - 1) as b:
                run(b)
            run(B - 1)
            run(B)
            run(B + 1)

        @block.sync
        def _(sp):
            def load_x(b):
                if not first(b):
                    sp.wait_ge(xT_ps, b)
                    carry(sp)
                sp.dma_start(x_t[:, :, :], x[b].rearrange("(t p) d -> p t d", p=P)).then_inc(x_in, 16)

            def load_residual(b):
                if not first(b):
                    sp.wait_ge(r1_done, b)
                    carry(sp)
                sp.dma_start(x_r[:, :, :], x[b].rearrange("(t p) d -> p t d", p=P)).then_inc(xr_in, 16)

            def store_parts(s):
                sp.wait_ge(part2, s + 1)
                carry(sp)
                sp.wait_ge(part1, s + 1)
                carry(sp)
                if not first(s):
                    sp.wait_ge(stacked[0], s * STACK)
                    carry(sp)
                    sp.wait_ge(stacked[1], s * STACK)
                    carry(sp)
                sp.dma_start(scratch.rearrange("a c p n -> p a c n"), parts[:, :, :, :]).then_inc(scr_out, 16)

            def stack_parts(s, half):
                sp.wait_ge(scr_out, s * 16 + 16)
                carry(sp)
                if not first(s):
                    sp.wait_ge(st_ps, (s - 1) * NB + (half + 1) * NB // 2)
                    carry(sp)
                for k, both in enumerate(SLOTS):
                    for c, part in enumerate(both):
                        sp.dma_start(stack[DK * k:DK * k + DK, c, half * HH:(half + 1) * HH, :],
                                     scratch[part, c].rearrange("(d h) n -> d h n", h=H)[:, half * HH:(half + 1) * HH, :])\
                          .then_inc(stacked[half], 16)

            def stack_maxima(s, half):
                sp.wait_ge(max_split, 2 * s + half + 1)
                carry(sp)
                for a in range(3):
                    sp.dma_start(stack[KZ + a:KZ + a + 1, 0, half * HH:(half + 1) * HH, :]
                                 .rearrange("o h (t q) -> o (h t) q", q=P), mparts[:, a, :]).then_inc(max_in, 16)

            sp.dma_start(ident_sb[:, :], ident).then_inc(ident_in, 16)
            load_x(0)
            for dst, src in ((wq_sb, wq), (wk_sb, wk)):
                sp.dma_start(dst[:, :], src).then_inc(qk_in, 16)
            for dst, src in ((cos_sb, cos), (sin_sb, sin), (mask_f, mask),
                             (wv_sb, wv), (wo_sb, wo), (router_sb, router)):
                sp.dma_start(dst[:, :], src).then_inc(first_in, 16)
            store_parts(0)
            sp.wait_ge(setup_v, 7)
            stack_parts(0, 0)
            stack_parts(0, 1)
            sp.dma_start(iota_sb[:, :], iota).then_inc(w_in, 16)
            sp.dma_start(bias_sb[:, :], bias.rearrange("(o e) -> o e", o=1).broadcast_to([P, E])).then_inc(w_in, 16)
            for room, _, _, src in staged:
                sp.dma_start(room, src).then_inc(w_in, 16)
            for c in range(HALVES):
                sp.dma_start(w2_sb[:, 0:E, c, :], w2[:, c * P:(c + 1) * P, :].rearrange("e p d -> p e d")).then_inc(w_in, 16)
            sp.dma_start(w2_sb[:, E, :, :], sw2[0].rearrange("(c p) d -> p c d", p=P)).then_inc(w_in, 16)
            stack_maxima(0, 0)

            def run(b):
                following, current, previous, oldest = [not isinstance(b, int) or 0 <= b - lag < B for lag in (-1, 0, 1, 2)]
                if following:
                    load_x(b + 1)
                if previous:
                    load_residual(b - 1)
                if current and not first(b):
                    stack_parts(b, 1)
                if following:
                    store_parts(b + 1)
                if oldest:
                    sp.wait_ge(y_sb_done, (b - 2) * T + T)
                    carry(sp)
                    sp.dma_start(out[b - 2].rearrange("(t p) d -> p t d", p=P), y_sb[:, :, :]).then_inc(out_done, 16)
                if current:
                    stack_maxima(b, 1)
                if following:
                    stack_parts(b + 1, 0)
                    stack_maxima(b + 1, 0)

            run(0)
            later_passes(sp, run)
            sp.wait_ge(out_done, 16 * (B + 1))
            carry(sp)

        @block.gpsimd
        def _(pool):
            pool.memset(minus_half[:, :], -0.5).then_inc(setup_p, 1)
            pool.memset(va[:, :, :, :], 0.0).then_inc(setup_p, 1)
            pool.wait_ge(setup_p, 2)
            pool.memset(va[:, :, :, DK:DK + 1], 1.0).then_inc(setup_p, 1)
            pool.wait_ge(setup_p, 3)
            pool.memset(rstd[:, 0:1], 0.0).then_inc(scaled_done, 1)
            pool.memset(rstd[:, 1:2], 0.0).then_inc(out_done, 16)
            pool.memset(rstd[:, 2:3], 0.0).then_inc(acc_done, 1)
            pool.memset(rstd[:, 3:4], 0.0).then_inc(hid_done, 1)
            pool.memset(rstd2[:, 0:1], 0.0).then_inc(gate_done, 1)

            def mask_unit(b, v):
                pool.wait_ge(exp_done, b * NB + v + 1)
                carry(pool)
                blocks = PAIR_UNITS[v % NU]
                if len(blocks) == 2:
                    step = blocks[1][2]
                    area = probs[:, v % PRING, 0:step + P]
                    area = bass.AP(area.tensor, area.offset, [list(area.ap[0]), [step, 2], [1, P]])
                    pattern = [[0, 2], [1, P]]
                else:
                    area, pattern = probs[:, v % PRING, 0:P], [[1, P]]
                pool.affine_select(out=area, in_=area, compare_op=ALU.is_ge, fill=0.0, base=0,
                                   pattern=pattern, channel_multiplier=-1).then_inc(masked, 1)

            def add_expert(f, e):
                pool.wait_ge(scaled_done, f * NE + e + 2)
                pool.wait_ge(acc_done, f * NE + e + 1)
                pool.tensor_tensor(acc[:, :, :], x1[:, :, :] if e == 0 else acc[:, :, :],
                                   scaled[:, e % 2, :, :], ALU.add).then_inc(acc_done, 1)

            def rope_sum(s):
                pool.wait_ge(m_used, project_use(s, 3) + 1)
                pool.tensor_tensor(qk[:, :, :], qk[:, :, :], rest[:, :, :], ALU.add).then_inc(qk_sb, 1)

            def split_rest(s):
                pool.wait_ge(part0, s + 1)
                pool.tensor_tensor(rest[:, :, :], qk[:, :, :], parts[:, 0, :, :], ALU.subtract).then_inc(rest_done, 1)

            def split_low(s):
                pool.wait_ge(part1, s + 1)
                pool.tensor_tensor(parts[:, 2, :, :], rest[:, :, :], parts[:, 1, :, :], ALU.subtract).then_inc(part2, 1)

            def run(b):
                for kind, n, lag in steps(b):
                    s = b - lag
                    if kind == "scores":
                        mask_unit(s, n)
                    elif kind == "rope":
                        rope_sum(s)
                    elif kind == "rest":
                        split_rest(s)
                    elif kind == "low":
                        split_low(s)
                    elif kind == "scale":
                        add_expert(s, n)
                    elif kind == "ln1":
                        pool.wait_ge(var1, s + 1)
                        pool.tensor_tensor(rstd[:, :], veps[:, :], minus_half[:, :], ALU.pow).then_inc(rstd1_done, 1)
                    elif kind == "ln2":
                        pool.wait_ge(var2, s + 1)
                        pool.tensor_tensor(rstd2[:, :], veps2[:, :], minus_half[:, :], ALU.pow).then_inc(rstd2_done, 1)

            rope_sum(0)
            split_rest(0)
            split_low(0)
            run(0)
            pool.wait_ge(w_in, 16 * W_LOADS)
            for n, (w, high, low, _) in enumerate(staged):
                pool.wait_ge(w_hi, n + 1)
                pool.tensor_tensor(low, w, high.bitcast(F32), ALU.subtract).then_inc(w_lo, 1)
            later_passes(pool, run)

        @block.scalar
        def _(act):
            def exp_unit(b, v):
                act.wait_ge(st_ps, b * NB + v + 1)
                if v >= PRING:
                    act.wait_ge(pv_ps, b * GROUPS + (v - PRING) // UPG + 1)
                elif not first(b):
                    act.wait_ge(pv_ps, (b - 1) * GROUPS + (v + NB - PRING) // UPG + 1)
                act.activation(probs[:, v % PRING, :], ps[:, SC + v % 2, :], ACT.Exp, scale=SCALE).then_inc(exp_done, 1)

            def copy_xT(b):
                act.wait_ge(xT_ps, b + 1)
                if not first(b):
                    act.wait_ge(v_ps, b)
                act.activation(xT[:, :], ps[:, PV, :], ACT.Copy).then_inc(xT_sb, 1)

            def split_high(b):
                if not first(b):
                    act.wait_ge(scr_out, b * 16)
                act.wait_ge(qk_sb, b + 1)
                act.activation(parts[:, 0, :, :], qk[:, :, :], ACT.Copy).then_inc(part0, 1)

            def split_mid(b):
                act.wait_ge(rest_done, b + 1)
                act.activation(parts[:, 1, :, :], rest[:, :, :], ACT.Copy).then_inc(part1, 1)

            def store_v(b):
                if not first(b):
                    act.wait_ge(pv_ps, b * GROUPS)
                act.wait_ge(v_ps, b + 1)
                act.activation(va[:, :, :, 0:DK], ps[:, PV, :].rearrange("p (t h d) -> p t h d", t=T, h=H),
                               ACT.Copy).then_inc(va_sb, 1)

            def half_tanh(f, c):
                act.wait_ge(g_ps, f * CH + c + 1)
                if not (first(f) and c < 2):
                    act.wait_ge(gate_done, f * CH + c)
                act.activation(th[:, c % 2, :], ps[:, gate_bank(f, c), :], ACT.Tanh, scale=0.5).then_inc(th_done, 1)

            def run(b):
                for kind, n, lag in steps(b):
                    s = b - lag
                    if kind == "scores":
                        exp_unit(s, n)
                    elif kind == "x_T":
                        copy_xT(s)
                    elif kind == "rope":
                        split_high(s)
                    elif kind == "rest":
                        split_mid(s)
                    elif kind == "v":
                        store_v(s)
                    elif kind == "out":
                        act.wait_ge(onT_ps, s + 1)
                        act.activation(onT[:, :], ps[:, PV, :], ACT.Copy).then_inc(onT_sb, 1)
                    elif kind == "x1_T":
                        act.wait_ge(x1T_ps, s + 1)
                        act.activation(x1T[:, :], ps[:, PV, :], ACT.Copy).then_inc(x1T_sb, 1)
                    elif kind == "weights":
                        act.wait_ge(gap_done, s + 1)
                        act.activation(egap[:, :], gap[:, :], ACT.Exp).then_inc(egap_done, 1)
                    elif kind == "tanh":
                        half_tanh(s, n)

            act.wait_ge(setup_p, 3)
            copy_xT(0)
            split_high(0)
            split_mid(0)
            run(0)
            later_passes(act, run)

        @block.tensor
        def _(pe):
            def x_transposes(s):
                pe.wait_ge(x_in, s * 16 + 16)
                if not first(s):
                    pe.wait_ge(va_sb, s)
                for t in range(T):
                    last = pe.transpose(ps[:, PV, t * P:(t + 1) * P], x_t[:, t, :], ident_sb[:, :])
                last.then_inc(xT_ps, 1)

            def project(s, c):
                if c == 0:
                    pe.wait_ge(xT_sb, s + 1)
                for n, w in enumerate(((wq_sb, wqr_sb), (wk_sb, wkr_sb))[c]):
                    use = project_use(s, 2 * c + n)
                    if not (first(s) and c == 0):
                        pe.wait_ge(m_used, use - 1)
                    pe.matmul(ps[:, M + n, :], w[:, :], xT[:, :], start=True, stop=True).then_inc(m_filled, 1)

            def project_v(s):
                if first(s):
                    pe.wait_ge(max_split, 1)
                else:
                    pe.wait_ge(ot_sb, s * GROUPS)
                for t in range(T):
                    last = pe.matmul(ps[:, PV, t * P:(t + 1) * P], xT[:, t * P:(t + 1) * P], wv_sb[:, :],
                                     start=True, stop=True)
                last.then_inc(v_ps, 1)

            def max_unit(s, u):
                i, h0, n, stride = MAX_UNITS[u]
                if u % NAH == 0:
                    pe.wait_ge(stacked[u // NAH], s * STACK + STACK)
                pe.wait_ge(m_used, max_use(s, u) - 1)
                unit = ps[:, M + u % 2, :]
                for k in range(n):
                    at = k * stride
                    w = (i + 1) * P
                    pe.matmul(unit[:, at:at + w], stack[0:KZ, 0, h0 + k, i * P:(i + 1) * P],
                              stack[0:KZ, 1, h0 + k, 0:w], start=True, stop=False)
                    last = pe.matmul(unit[:, at + w - P:at + w], ident_bf[:, :], mask_bf[:, :],
                                     start=False, stop=True)
                last.then_inc(m_filled, 1)

            def max_rows(s, half):
                pe.wait_ge(m_used, max_use(s, half * NAH + NAH - 1) + 1)
                if half == 1:
                    pe.wait_ge(ot_sb, s * GROUPS + 1)
                elif not first(s):
                    pe.wait_ge(ot_sb, s * GROUPS - 1)
                carry(pe)
                pe.transpose(ps[0:HH * T, PV, 0:P], negmax[:, half * HH:(half + 1) * HH, :].rearrange("p h t -> p (h t)"),
                             ident_sb[:, :]).then_inc(maxT_ps, 1)

            def scores_unit(s, v):
                if v % (NB // 2) == 0:
                    pe.wait_ge(max_in, (2 * s + v // (NB // 2) + 1) * 48)
                if not (first(s) and v < 2):
                    pe.wait_ge(exp_done, s * NB + v - 1)
                unit = ps[:, SC + v % 2, :]
                for k, j, at in PAIR_UNITS[v % NU]:
                    h = 2 * (v // NU) + k
                    last = pe.matmul(unit[:, at:at + S - j * P], stack[0:KM, 1, h, j * P:(j + 1) * P],
                                     stack[0:KM, 0, h, j * P:S], start=True, stop=True)
                last.then_inc(st_ps, 1)

            def weighted_values(s, g):
                pe.wait_ge(masked, s * NB + UPG * (g + 1))
                if g == 0:
                    pe.wait_ge(va_sb, s + 1)
                    if not first(s):
                        pe.wait_ge(x1T_sb, s)
                    else:
                        pe.wait_ge(xT_sb, 2)
                elif g == 1:
                    pe.wait_ge(max_split, 2 * s + 2)
                elif g == 3 and not last_one(s):
                    pe.wait_ge(max_split, 2 * s + 3)
                else:
                    pe.wait_ge(ot_sb, s * GROUPS + g)
                for j in range(T):
                    for k in range(PER_PV):
                        n, at = next((n, at) for n, unit in enumerate(PAIR_UNITS)
                                     for kk, jj, at in unit if (kk, jj) == (k % 2, j))
                        v = UPG * g + NU * (k // 2) + n
                        last = pe.matmul(ps[32 * k:32 * k + 32, PV, j * P:S], va[:, j, PER_PV * g + k, :],
                                         probs[:, v % PRING, at:at + S - j * P], start=(j == 0), stop=(j == T - 1),
                                         skip_group_check=True)
                last.then_inc(pv_ps, 1)

            def heads_transposes(s, pair):
                pe.wait_ge(ot_sb, s * GROUPS + GROUPS)
                for t in (2 * pair, 2 * pair + 1):
                    pe.wait_ge(m_used, heads_use(s, t) - 1)
                    for g in range(GROUPS):
                        last = pe.transpose(ps[:, M + t % 2, g * P:(g + 1) * P], ot[:, g, t * P:(t + 1) * P], ident_sb[:, :])
                    last.then_inc(m_filled, 1)

            def out_transposes(s):
                if last_one(s):
                    pe.wait_ge(ot_sb, s * GROUPS + GROUPS)
                elif isinstance(s, int) and s == B - 2:
                    pe.wait_ge(va_sb, s + 2)
                else:
                    pe.wait_ge(xT_sb, s + 3)
                for t in range(T):
                    pe.wait_ge(m_used, heads_use(s, t) + 1)
                    last = pe.transpose(ps[:, PV, t * P:(t + 1) * P], on[:, t, :], ident_sb[:, :])
                last.then_inc(onT_ps, 1)

            def project_out(s):
                pe.wait_ge(onT_sb, s + 1)
                for t in range(T):
                    last = pe.matmul(ps[:, PV, t * P:(t + 1) * P], onT[:, t * P:(t + 1) * P], wo_sb[:, :],
                                     start=True, stop=True)
                last.then_inc(wo_ps, 1)

            def x1_transposes(f):
                for t in range(T):
                    pe.wait_ge(x1_sb, f * T + t + 1)
                    last = pe.transpose(ps[:, PV, t * P:(t + 1) * P], x1[:, t, :], ident_sb[:, :])
                last.then_inc(x1T_ps, 1)

            def route(f):
                pe.wait_ge(x1T_sb, f + 1)
                pe.wait_ge(scaled_done, f * NE + 1)
                for t in range(T):
                    last = pe.matmul(ps[:, Y, t * E:(t + 1) * E], x1T[:, t * P:(t + 1) * P], router_sb[:, :],
                                     start=True, stop=True)
                last.then_inc(logit_ps, 1)

            def first_products(bank, w_high, w_low, c):
                e, half = c // HALVES, c % HALVES
                parts_of = ((w_high, x1T_hi), (w_high, x1T_lo), (w_low, x1T_hi))
                for n, (w, x1) in enumerate(parts_of):
                    last = pe.matmul(ps[:, bank, :], w[:, e, half * P:(half + 1) * P], x1[:, :],
                                     start=(n == 0), stop=(n == len(parts_of) - 1))
                return last

            def up_gate(f, c):
                if c == 0:
                    pe.wait_ge(x1T_low, f + 1)
                    if first(f):
                        pe.wait_ge(w_lo, len(staged))
                if two_banks(f) and c == 1:
                    pe.wait_ge(exp_done, NB * B)
                pe.wait_ge(gate_done, f * CH + c + (0 if two_banks(f) and c > 0 else 1))
                first_products(gate_bank(f, c), w1_hi, w1_lo, c).then_inc(g_ps, 1)

            def up(f, c):
                pe.wait_ge(hid_done, f * CH + c + (0 if two_banks(f) and c > 0 else 1))
                first_products(gate_bank(f, c) + 1, w3_hi, w3_lo, c).then_inc(u_ps, 1)

            def down(f, e):
                pe.wait_ge(hid_done, f * CH + HALVES * (e + 1) + 1)
                if e == 0:
                    pe.wait_ge(logits_sb, f + 1)
                else:
                    pe.wait_ge(scaled_done, f * NE + e + 1)
                for t in range(T):
                    for half in range(HALVES):
                        c = e * HALVES + half
                        last = pe.matmul(ps[:, Y, t * P:(t + 1) * P], hid[:, c % 4, t * P:(t + 1) * P],
                                         w2_sb[:, e, half, :], start=(half == 0), stop=(half == HALVES - 1))
                last.then_inc(y_ps, 1)

            def run(b):
                for kind, n, lag in steps(b):
                    s = b - lag
                    if kind == "max":
                        max_unit(s, n)
                    elif kind == "max_rows":
                        max_rows(s, n)
                    elif kind == "scores":
                        scores_unit(s, n)
                    elif kind == "values":
                        weighted_values(s, n)
                    elif kind == "x_T":
                        x_transposes(s)
                    elif kind == "project":
                        project(s, n)
                    elif kind == "v":
                        project_v(s)
                    elif kind == "heads_T":
                        heads_transposes(s, n)
                    elif kind == "out_T":
                        out_transposes(s)
                    elif kind == "out":
                        project_out(s)
                    elif kind == "x1_T":
                        x1_transposes(s)
                    elif kind == "router":
                        route(s)
                    elif kind == "gate":
                        up_gate(s, n)
                    elif kind == "up":
                        up(s, n)
                    elif kind == "down":
                        down(s, n)

            pe.wait_ge(ident_in, 16)
            x_transposes(0)
            pe.wait_ge(qk_in, 32)
            pe.wait_ge(setup_v, 4)
            project(0, 0)
            project(0, 1)
            pe.wait_ge(setup_v, 9)
            pe.wait_ge(setup_p, 3)
            pe.wait_ge(first_in, 16 * FIRST_LOADS)
            for u in range(NAH):
                max_unit(0, u)
            max_rows(0, 0)
            run(0)
            pe.wait_ge(w_in, 16 * W_LOADS)
            later_passes(pe, run)

        @block.vector
        def _(dve):
            dve.wait_ge(qk_in, 32)
            for src, dst in ((wq_sb, wqr_sb), (wk_sb, wkr_sb)):
                s4 = src[:, :].rearrange("p (a e h) -> p a e h", e=2, h=H)
                d4 = dst[:, :].rearrange("p (a e h) -> p a e h", e=2, h=H)
                dve.tensor_scalar(d4[:, :, 0, :], s4[:, :, 1, :], -1.0, None, ALU.mult).then_inc(setup_v, 1)
                dve.tensor_copy(d4[:, :, 1, :], s4[:, :, 0, :]).then_inc(setup_v, 1)

            def link(ins, semaphore, value):
                ins.then_inc(semaphore, 1)
                dve.wait_ge(semaphore, value)

            def rope_products(s, c):
                if not first(s):
                    dve.wait_ge(part2, s)
                for n, (dst, table) in enumerate(((qk, cos_sb), (rest, sin_sb))):
                    dve.wait_ge(m_filled, project_use(s, 2 * c + n) + 1)
                    dve.tensor_tensor(dst[:, c, :], ps[:, M + n, :], table[:, :], ALU.mult).then_inc(m_used, 1)

            def max_unit(s, u):
                i, h0, n, stride = MAX_UNITS[u]
                dve.wait_ge(m_filled, max_use(s, u) + 1)
                unit = ps[:, M + u % 2, :].rearrange("p (h s) -> p h s", s=stride)
                dve.tensor_reduce(negmax[:, h0:h0 + n, i], unit[:, :, 0:(i + 1) * P], AX_X, ALU.max,
                                  negate=True).then_inc(m_used, 1)

            def split_max(s, half):
                k = 2 * s + half
                dve.wait_ge(maxT_ps, k + 1)
                mT = ps[0:HH * T, PV, 0:P]
                link(dve.tensor_copy(mparts[:, 0, :], mT), max_chain, 3 * k + 1)
                link(dve.tensor_tensor(mrest[:, :], mT, mparts[:, 0, :], ALU.subtract), max_chain, 3 * k + 2)
                link(dve.tensor_copy(mparts[:, 1, :], mrest[:, :]), max_chain, 3 * k + 3)
                dve.tensor_tensor(mparts[:, 2, :], mrest[:, :], mparts[:, 1, :], ALU.subtract).then_inc(max_split, 1)

            def values_out(s, g):
                dve.wait_ge(pv_ps, s * GROUPS + g + 1)
                dve.tensor_copy(ot[:, g, :], ps[:, PV, :]).then_inc(ot_sb, 1)

            def normalize(s, pair):
                tiles = (2 * pair, 2 * pair + 1)
                for t in tiles:
                    dve.wait_ge(m_filled, heads_use(s, t) + 1)
                    oq = ps[:, M + t % 2, :].rearrange("p (h c) -> p h c", c=32)
                    ins = dve.reciprocal(rden[:, t, :], oq[:, :, DK])
                link(ins, rden_done, 2 * s + pair + 1)
                for t in tiles:
                    oq = ps[:, M + t % 2, :].rearrange("p (h c) -> p h c", c=32)
                    dve.tensor_tensor(on[:, t, :].rearrange("p (h d) -> p h d", d=DK), oq[:, :, 0:DK],
                                      rden[:, t, :].rearrange("p (h o) -> p h o", o=1).broadcast_to([P, H, DK]),
                                      ALU.mult).then_inc(m_used, 1)

            def layernorm_stats(b, src, st, m, ve, chain, var_sem):
                for t in range(T):
                    ins = dve.bn_stats(st[:, t, :], src[:, t, :])
                link(ins, chain, 2 * b + 1)
                carry(dve)
                for t in range(T):
                    ins = dve.bn_aggr(m[:, t, :], st[:, t, :])
                link(ins, chain, 2 * b + 2)
                dve.tensor_scalar(ve[:, :], m[:, :, 1], EPS, None, ALU.add).then_inc(var_sem, 1)

            def layernorm_end(b, src, m, rs, rstd_sem, dst, dst_sem):
                dve.wait_ge(rstd_sem, b + 1)
                for t in range(T):
                    dve.tensor_scalar(dst[:, t, :], src[:, t, :], m[:, t, 0:1], rs[:, t:t + 1],
                                      ALU.subtract, ALU.mult).then_inc(dst_sem, 1)

            def layernorm1_stats(b):
                dve.wait_ge(wo_ps, b + 1)
                dve.wait_ge(xr_in, b * 16 + 16)
                link(dve.tensor_tensor(r1[:, :, :], x_r[:, :, :], ps[:, PV, :].rearrange("p (t d) -> p t d", t=T), ALU.add),
                     r1_done, b + 1)
                layernorm_stats(b, r1, stats, mv, veps, ln1_chain, var1)

            def layernorm1_end(b):
                if not first(b):
                    dve.wait_ge(acc_done, (b - 1) * NE + 2)
                layernorm_end(b, r1, mv, rstd, rstd1_done, x1, x1_sb)

            def route(f):
                step = [ROUTE * f]

                def step_on(ins):
                    step[0] = step[0] + 1
                    link(ins, route_chain, step[0])

                dve.wait_ge(logit_ps, f + 1)
                link(dve.tensor_tensor(logits[:, :, :], ps[:, Y, 0:T * E].rearrange("p (t e) -> p t e", t=T),
                                       bias_sb[:, :].rearrange("p (o e) -> p o e", o=1).broadcast_to([P, T, E]), ALU.add),
                     logits_sb, f + 1)
                carry(dve)
                for t in range(T):
                    ins = dve.max(top[:, t, :], logits[:, t, :])
                step_on(ins)
                carry(dve)
                for t in range(T):
                    ins = dve.max_index(topi[:, t, :], top[:, t, :], logits[:, t, :])
                dve.tensor_tensor(gap[:, :], top[:, :, 1], top[:, :, 0], ALU.subtract).then_inc(gap_done, 1)
                step_on(ins)
                step_on(dve.tensor_copy(topf[:, :, :], topi[:, :, 0:2]))

            def route_weights(f):
                step = [ROUTE * f + 3]

                def step_on(ins):
                    step[0] = step[0] + 1
                    link(ins, route_chain, step[0])

                dve.wait_ge(egap_done, f + 1)
                step_on(dve.tensor_scalar(den2[:, :], egap[:, :], 2.0, 2.0, ALU.mult, ALU.add))
                step_on(dve.reciprocal(rw[:, :, 0], den2[:, :]))
                step_on(dve.tensor_tensor(rw[:, :, 1], rw[:, :, 0], egap[:, :], ALU.mult))
                for n, eq in enumerate((eq0, eq1)):
                    ins = dve.tensor_tensor(eq[:, :, :], iota_sb[:, :].rearrange("p (o e) -> p o e", o=1).broadcast_to([P, T, E]),
                                            topf[:, :, n:n + 1].broadcast_to([P, T, E]), ALU.is_equal)
                step_on(ins)
                for n, eq in enumerate((eq0, eq1)):
                    ins = dve.tensor_tensor(eq[:, :, :], eq[:, :, :], rw[:, :, n:n + 1].broadcast_to([P, T, E]), ALU.mult)
                step_on(ins)
                dve.tensor_tensor(cw[:, :, 0:E], eq0[:, :, :], eq1[:, :, :], ALU.add)
                step_on(dve.memset(cw[:, :, E:NE], 0.5))

            ROUTE = 9

            def split_x1T(f):
                dve.wait_ge(x1T_sb, f + 1)
                link(dve.tensor_copy(x1T_hi[:, :], x1T[:, :]), x1T_high, f + 1)
                dve.tensor_tensor(x1T_lo[:, :], x1T[:, :], x1T_hi[:, :].bitcast(F32), ALU.subtract).then_inc(x1T_low, 1)

            def gated(f, c):
                dve.wait_ge(th_done, f * CH + c + 1)
                link(dve.scalar_tensor_tensor(out=gate[:, c % 2, :], in0=th[:, c % 2, :], scalar=1.0, in1=ps[:, gate_bank(f, c), :],
                                              op0=ALU.add, op1=ALU.mult), gate_done, f * CH + c + 2)
                dve.wait_ge(u_ps, f * CH + c + 1)
                if c >= 4:
                    dve.wait_ge(y_ps, f * NE + (c - 4) // HALVES + 1)
                dve.tensor_tensor(hid[:, c % 4, :], gate[:, c % 2, :], ps[:, gate_bank(f, c) + 1, :], ALU.mult).then_inc(hid_done, 1)

            def scale_expert(f, e):
                dve.wait_ge(y_ps, f * NE + e + 1)
                if e >= 2:
                    dve.wait_ge(acc_done, f * NE + e)
                dve.tensor_tensor(scaled[:, e % 2, :, :], ps[:, Y, :].rearrange("p (t d) -> p t d", t=T),
                                  cw[:, :, e:e + 1].broadcast_to([P, T, D]), ALU.mult).then_inc(scaled_done, 1)

            def layernorm2_stats(f):
                dve.wait_ge(acc_done, f * NE + NE + 1)
                layernorm_stats(f, acc, stats2, mv2, veps2, ln2_chain, var2)

            def layernorm2_end(f):
                dve.wait_ge(out_done, f * 16 + 16)
                layernorm_end(f, acc, mv2, rstd2, rstd2_done, y_sb, y_sb_done)

            def run(b):
                for kind, n, lag in steps(b):
                    s = b - lag
                    if kind == "max":
                        max_unit(s, n)
                    elif kind == "max_rows":
                        split_max(s, n)
                    elif kind == "values":
                        values_out(s, n)
                    elif kind == "project":
                        rope_products(s, n)
                    elif kind == "norm":
                        normalize(s, n)
                    elif kind == "ln1_stats":
                        layernorm1_stats(s)
                    elif kind == "ln1":
                        layernorm1_end(s)
                    elif kind == "router":
                        route(s)
                    elif kind == "weights":
                        route_weights(s)
                    elif kind == "x1_split":
                        split_x1T(s)
                    elif kind == "glu":
                        gated(s, n)
                    elif kind == "scale":
                        scale_expert(s, n)
                    elif kind == "ln2_stats":
                        layernorm2_stats(s)
                    elif kind == "ln2":
                        layernorm2_end(s)

            dve.wait_ge(first_in, 16 * FIRST_LOADS)
            rope_products(0, 0)
            rope_products(0, 1)
            dve.wait_ge(ident_in, 16)
            dve.tensor_copy(ident_bf[:, :], ident_sb[:, :]).then_inc(setup_v, 1)
            dve.tensor_copy(mask_bf[:, :], mask_f[:, :]).then_inc(setup_v, 1)
            dve.memset(stack[32:64, :, :, :], 0.0).then_inc(setup_v, 1)
            dve.memset(stack[64:KZ, :, :, :], 0.0).then_inc(setup_v, 1)
            dve.memset(stack[KZ:KM, 1, :, :], 1.0).then_inc(setup_v, 1)
            for u in range(NAH):
                max_unit(0, u)
            split_max(0, 0)
            run(0)
            dve.wait_ge(w_in, 16 * W_LOADS)
            for w, high, _, _ in staged:
                dve.tensor_copy(high, w).then_inc(w_hi, 1)
            later_passes(dve, run)


_INS = ["x", "wq", "wk", "wv", "wo", "cos", "sin", "ident", "mask", "iota", "router", "bias",
        "w1", "w3", "w2", "sw1", "sw3", "sw2"]


def kernel(L0_attn_x, L0_attn_Wq, L0_attn_Wk, L0_attn_Wv, L0_attn_Wo, L0_ffn_router_w, L0_ffn_experts_bias,
           L0_ffn_w1, L0_ffn_w3, L0_ffn_w2, L0_ffn_sw1, L0_ffn_sw3, L0_ffn_sw2):
    import numpy as np
    import concourse.bacc as bacc
    from concourse.bass_utils import run_bass_kernel_spmd

    B, S, D = L0_attn_x.shape
    H, E = 16, L0_ffn_w1.shape[0]
    dk = D // H
    inv_freq = (1.0 / 10000.0 ** (np.arange(0, dk, 2, dtype=np.float32) / np.float32(dk))).astype(np.float32)
    angles = np.outer(np.arange(S, dtype=np.float32), inv_freq).astype(np.float32)
    table = lambda f: np.repeat(np.repeat(f(angles).astype(np.float32), 2, axis=1).T, H, axis=0)
    by_dim = lambda w: np.asarray(w).reshape(D, H, dk).transpose(0, 2, 1).reshape(D, D)
    arrays = {
        "x": L0_attn_x, "wq": by_dim(L0_attn_Wq), "wk": by_dim(L0_attn_Wk), "wv": L0_attn_Wv, "wo": L0_attn_Wo,
        "cos": table(np.cos), "sin": table(np.sin), "ident": np.eye(P, dtype=np.float32),
        "mask": np.triu(np.full((P, P), NEG, np.float32), 1),
        "iota": np.tile(np.arange(E, dtype=np.float32), (P, 1)),
        "router": np.asarray(L0_ffn_router_w).T, "bias": L0_ffn_experts_bias,
        "w1": L0_ffn_w1, "w3": L0_ffn_w3, "w2": L0_ffn_w2, "sw1": L0_ffn_sw1, "sw3": L0_ffn_sw3, "sw2": L0_ffn_sw2,
    }
    arrays = {f"in_{k}": np.ascontiguousarray(v) for k, v in arrays.items()}
    nc = bacc.Bacc("TRN2", target_bir_lowering=False, num_devices=1)
    args = [nc.dram_tensor(f"in_{k}", arrays[f"in_{k}"].shape, mybir.dt.from_np(arrays[f"in_{k}"].dtype),
                           kind="ExternalInput").ap() for k in _INS]
    out = nc.dram_tensor("out", (B, S, D), F32, kind="ExternalOutput").ap()
    build_block(nc, *args, out)
    r = run_bass_kernel_spmd(nc, [arrays], core_ids=[0])
    return r.results[0]["out"]
```
